# Optimizing a Trainium2 kernel written in Bass

```python
import numpy as np
import jax
import jax.numpy as jnp

def _softmax(x, axis=-1):
    return jax.nn.softmax(x, axis=axis)

def _gelu(x):
    return jax.nn.gelu(x, approximate=True)

def _silu(x):
    return jax.nn.silu(x)

def _sigmoid(x):
    return jax.nn.sigmoid(x)

def _layernorm(x, axis=-1, eps=1e-05):
    m = jnp.mean(x, axis=axis, keepdims=True)
    v = jnp.var(x, axis=axis, keepdims=True)
    return (x - m) / jnp.sqrt(v + eps)

def _scatter_add(tgt, idx, src, axis=0):
    return tgt.at[idx].add(src)

def _segment_sum(src, seg, n):
    return jax.ops.segment_sum(src, seg, n)
kernel_name = 'mk_gnn_resnorm_d2_gnn_r8_c857b2'

def setup_inputs(seed: int=0):
    np.random.seed(seed)
    _w = jnp.asarray

    def _rec_inputs():
        import jax
        import jax.numpy as jnp
        _gk = jax.random.key(seed)
        x = -0.0003713 + 1 * jax.random.normal(jax.random.fold_in(_gk, 1), (12500, 128), jnp.float32)
        src = jax.random.randint(jax.random.fold_in(_gk, 2), (200000,), 0, 12500, jnp.int32)
        dst = jax.random.randint(jax.random.fold_in(_gk, 3), (200000,), 0, 12500, jnp.int32)
        _o = jnp.argsort(dst, stable=True)
        src = src[_o]
        dst = dst[_o]
        edge_weight = jax.random.uniform(jax.random.fold_in(_gk, 12), (200000,), jnp.float32, 0.0, 0.999998)
        return (x, src, dst, edge_weight)
    x, src, dst, edge_weight = _rec_inputs()

    def _L0_gnn_setup():
        import jax, jax.numpy as jnp
        import numpy as np
        N_NODES = 12500
        N_EDGES = 80000
        DIM = 128
        key = jax.random.key(seed)
        k1, k2, k3, k4, k5 = jax.random.split(key, 5)
        x = jax.random.normal(k1, (N_NODES, DIM), dtype=jnp.float32)
        edge_index = jax.random.randint(k2, (2, N_EDGES), 0, N_NODES, dtype=jnp.int64)
        edge_weight = jax.random.uniform(k3, (N_EDGES,), dtype=jnp.float32)
        W = jax.random.normal(k4, (DIM, DIM), dtype=jnp.float32) * (1.0 / np.sqrt(DIM))
        b = jax.random.normal(k5, (DIM,), dtype=jnp.float32) * 0.01
        return {'x': x, 'edge_index': edge_index, 'edge_weight': edge_weight, 'W': W, 'b': b}
    _L0_gnn_all = _L0_gnn_setup()
    _L0_gnn_in = {k: v for k, v in _L0_gnn_all.items() if k in ('W', 'b')}
    del _L0_gnn_all

    def _L1_gnn_setup():
        import jax, jax.numpy as jnp
        import numpy as np
        N, E, D, T, L, DMLP = (12500, 100000, 128, 4, 2, 512)
        FIN = D // T
        AVG_LOG = float(np.log(17.0))
        LN_EPS = 1e-05

        def _layer_norm(x, g, b):
            mu = x.mean(-1, keepdims=True)
            var = jnp.var(x, axis=-1, keepdims=True)
            return (x - mu) / jnp.sqrt(var + LN_EPS) * g + b
        ks = jax.random.split(jax.random.key(seed), 10)
        s = 0.05
        return {'x': jax.random.normal(ks[0], (N, D), jnp.float32), 'edge_index': jax.random.randint(ks[1], (2, E), 0, N, jnp.int64) if jax.config.jax_enable_x64 else jax.random.randint(ks[1], (2, E), 0, N, jnp.int32), 'ln1_g': jnp.ones((L, D), jnp.float32), 'ln1_b': jnp.zeros((L, D), jnp.float32), 'W_pre': s * jax.random.normal(ks[2], (L, T, 2 * FIN, FIN), jnp.float32), 'b_pre': jnp.zeros((L, T, FIN), jnp.float32), 'W_post': s * jax.random.normal(ks[3], (L, T, 13 * FIN, FIN), jnp.float32), 'b_post': jnp.zeros((L, T, FIN), jnp.float32), 'W_lin': s * jax.random.normal(ks[4], (L, D, D), jnp.float32), 'b_lin': jnp.zeros((L, D), jnp.float32), 'ln2_g': jnp.ones((L, D), jnp.float32), 'ln2_b': jnp.zeros((L, D), jnp.float32), 'W1': s * jax.random.normal(ks[5], (L, D, DMLP), jnp.float32), 'b1': jnp.zeros((L, DMLP), jnp.float32), 'W2': s * jax.random.normal(ks[6], (L, DMLP, D), jnp.float32), 'b2': jnp.zeros((L, D), jnp.float32)}
    _L1_gnn_all = _L1_gnn_setup()
    _L1_gnn_in = {k: v for k, v in _L1_gnn_all.items() if k in ('ln1_g', 'ln1_b', 'W_pre', 'b_pre', 'W_post', 'b_post', 'W_lin', 'b_lin', 'ln2_g', 'ln2_b', 'W1', 'b1', 'W2', 'b2')}
    del _L1_gnn_all
    return {'x': x, 'src': src, 'dst': dst, 'edge_weight': edge_weight, 'L0_gnn_W': _L0_gnn_in['W'], 'L0_gnn_b': _L0_gnn_in['b'], 'L1_gnn_ln1_g': _L1_gnn_in['ln1_g'], 'L1_gnn_ln1_b': _L1_gnn_in['ln1_b'], 'L1_gnn_W_pre': _L1_gnn_in['W_pre'], 'L1_gnn_b_pre': _L1_gnn_in['b_pre'], 'L1_gnn_W_post': _L1_gnn_in['W_post'], 'L1_gnn_b_post': _L1_gnn_in['b_post'], 'L1_gnn_W_lin': _L1_gnn_in['W_lin'], 'L1_gnn_b_lin': _L1_gnn_in['b_lin'], 'L1_gnn_ln2_g': _L1_gnn_in['ln2_g'], 'L1_gnn_ln2_b': _L1_gnn_in['ln2_b'], 'L1_gnn_W1': _L1_gnn_in['W1'], 'L1_gnn_b1': _L1_gnn_in['b1'], 'L1_gnn_W2': _L1_gnn_in['W2'], 'L1_gnn_b2': _L1_gnn_in['b2']}

def reference(x, src, dst, edge_weight, L0_gnn_W, L0_gnn_b, L1_gnn_ln1_g, L1_gnn_ln1_b, L1_gnn_W_pre, L1_gnn_b_pre, L1_gnn_W_post, L1_gnn_b_post, L1_gnn_W_lin, L1_gnn_b_lin, L1_gnn_ln2_g, L1_gnn_ln2_b, L1_gnn_W1, L1_gnn_b1, L1_gnn_W2, L1_gnn_b2):
    import jax
    import jax.numpy as jnp

    def _L0_gnn_ref(x, edge_index, edge_weight, W, b):
        import jax, jax.numpy as jnp
        import numpy as np
        N_NODES = 12500
        N_EDGES = 80000
        DIM = 128
        row, col = (edge_index[0], edge_index[1])
        msgs = edge_weight[:, None] * x[row]
        agg = jax.ops.segment_sum(msgs, col, num_segments=x.shape[0])
        return agg @ W.T + b

    def _L1_gnn_ref(x, edge_index, ln1_g, ln1_b, W_pre, b_pre, W_post, b_post, W_lin, b_lin, ln2_g, ln2_b, W1, b1, W2, b2):
        import jax, jax.numpy as jnp
        import numpy as np
        N, E, D, T, L, DMLP = (12500, 100000, 128, 4, 2, 512)
        FIN = D // T
        AVG_LOG = float(np.log(17.0))
        LN_EPS = 1e-05

        def _layer_norm(x, g, b):
            mu = x.mean(-1, keepdims=True)
            var = jnp.var(x, axis=-1, keepdims=True)
            return (x - mu) / jnp.sqrt(var + LN_EPS) * g + b
        n, d = x.shape
        src, dst = (edge_index[0], edge_index[1])
        cnt = jax.ops.segment_sum(jnp.ones(src.shape, x.dtype), dst, num_segments=n)
        deg = jnp.maximum(cnt, 1.0)
        amp = (jnp.log(deg + 1.0) / AVG_LOG)[:, None, None]
        att = (AVG_LOG / jnp.log(deg + 1.0))[:, None, None]
        has = (cnt > 0)[:, None, None]
        denom = deg[:, None, None]
        for l in range(ln1_g.shape[0]):
            h = _layer_norm(x, ln1_g[l], ln1_b[l]).reshape(n, T, FIN)
            m = jnp.concatenate([h[dst], h[src]], axis=-1)
            m = jnp.einsum('etf,tfg->etg', m, W_pre[l]) + b_pre[l]
            mean = jax.ops.segment_sum(m, dst, num_segments=n) / denom
            mean2 = jax.ops.segment_sum(m * m, dst, num_segments=n) / denom
            std = jnp.sqrt(jax.nn.relu(mean2 - mean * mean) + 1e-05)
            mn = jnp.where(has, jax.ops.segment_min(m, dst, num_segments=n), 0.0)
            mx = jnp.where(has, jax.ops.segment_max(m, dst, num_segments=n), 0.0)
            aggs = jnp.concatenate([mean, mn, mx, std], axis=-1)
            agg = jnp.concatenate([aggs, aggs * amp, aggs * att], -1)
            comb = jnp.concatenate([h, agg], axis=-1)
            o = jnp.einsum('ntf,tfg->ntg', comb, W_post[l]) + b_post[l]
            o = o.reshape(n, d) @ W_lin[l] + b_lin[l]
            x = x + o
            h2 = _layer_norm(x, ln2_g[l], ln2_b[l])
            h2 = jax.nn.gelu(h2 @ W1[l] + b1[l], approximate=False) @ W2[l] + b2[l]
            x = x + h2
        return x
    edge_index = jnp.stack([src, dst])
    x = _layernorm(x + _L0_gnn_ref(x, edge_index, edge_weight, L0_gnn_W, L0_gnn_b), axis=-1)
    x = _layernorm(x + _L1_gnn_ref(x, edge_index, L1_gnn_ln1_g, L1_gnn_ln1_b, L1_gnn_W_pre, L1_gnn_b_pre, L1_gnn_W_post, L1_gnn_b_post, L1_gnn_W_lin, L1_gnn_b_lin, L1_gnn_ln2_g, L1_gnn_ln2_b, L1_gnn_W1, L1_gnn_b1, L1_gnn_W2, L1_gnn_b2), axis=-1)
    return x

_drawn_inputs = setup_inputs


def setup_inputs(seed=0):
    import zlib

    import numpy as np

    out = dict(_drawn_inputs(seed))
    spreads = {'L1_gnn_ln1_g': (1.0, 0.2),
     'L1_gnn_ln1_b': (0.0, 0.435),
     'L1_gnn_b_pre': (0.0, 0.1),
     'L1_gnn_b_post': (0.0, 0.1),
     'L1_gnn_b_lin': (0.0, 0.1),
     'L1_gnn_ln2_g': (1.0, 0.2),
     'L1_gnn_ln2_b': (0.0, 0.288),
     'L1_gnn_b1': (0.0, 0.1),
     'L1_gnn_b2': (0.0, 0.1)}
    factors = {'L0_gnn_b': 8.0}
    for name, (base, spread) in spreads.items():
        noise = np.random.default_rng([zlib.crc32(name.encode()), seed]).standard_normal(out[name].shape)
        drawn = base * np.exp(spread * noise) if base else spread * noise
        out[name] = jnp.asarray(drawn.astype(out[name].dtype))
    for name, factor in factors.items():
        out[name] = (out[name] * factor).astype(out[name].dtype)
    return out
```

```python
import concourse.bass as bass
from concourse import mybir
from contextlib import ExitStack
import numpy as np

F32 = mybir.dt.float32
BF16 = mybir.dt.bfloat16
I32 = mybir.dt.int32
ALU = mybir.AluOpType
ACT = mybir.ActivationFunctionType
AX = mybir.AxisListType

P = 128
AVG_LOG = float(np.log(17.0))
EPS = 1e-5
BIG = 3.0e38


def gnn_kernel(nc, x, src, dst, edge_weight, W, b, ln1_g, ln1_b, W_pre, b_pre, W_post, b_post, W_lin, b_lin,
               ln2_g, ln2_b, W1, b1, W2, b2, out):
    N, D = x.shape
    E = src.shape[0]
    L, T, F2, F = W_pre.shape
    DM = W1.shape[2]
    MC = DM // P
    NB = -(-N // P)
    NP = NB * P
    LAST = N - (NB - 1) * P
    ZROW = NP
    EP = 125
    EC = E // EP
    CH = 400
    NCH = E // CH
    CPP = EC // CH
    RUN = 64
    RING = 32
    HALF = RING // 2
    AUX = 2 * RING
    QRT = 4
    SQR = 4
    NODEW = P * NB
    SMAX = E + E // P + 4 * NB + 4 * P + RING
    SMAX += (-SMAX) % 64 + 32
    GR = 7
    W_IN = 16 * (1 + L * (11 + MC + 3 * T))

    ctx = ExitStack()
    with ctx:
        def sb(name, shape, dt=F32):
            return ctx.enter_context(nc.sbuf_tensor(name, shape, dt))

        def pb(name, shape, dt=F32):
            return ctx.enter_context(nc.psum_tensor(name, shape, dt))

        def sem(name):
            return ctx.enter_context(nc.semaphore(name))

        def dram(name, shape, dt=F32):
            return nc.dram_tensor(name, shape, dt, kind="Internal").ap()

        tables = [dram("table_x", [ZROW + 1, D]), dram("table_b0", [ZROW + 1, D]), dram("table_b1", [ZROW + 1, D])]
        dst_rows = dram("dst_rows", [NCH, CH])
        pairs = dram("pairs", [E + RUN, 2], I32)
        node_info = dram("node_info", [NP, 4], I32)
        slot_idx = dram("slot_idx", [P, SMAX], I32)
        slot_aux = dram("slot_aux", [P, 2, SMAX])
        x0_rows = dram("x0_rows", [NB, P, D])
        pairs_e = pairs.rearrange("e (k o) -> (e k) o", o=1)

        X = sb("X", [P, NODEW])
        A = sb("A", [P, NODEW])
        B = sb("B", [P, NODEW])
        ring = sb("ring", [P, RING * D])
        sq_ring = sb("sq_ring", [P, SQR * D])
        idx_ring = sb("idx_ring", [P, RING], I32)
        aux_ring = sb("aux_ring", [P, AUX])
        bounds = sb("bounds", [1, 4 * NB + 1], I32)
        rounds = sb("rounds", [1, NB + 1], I32)
        totals = sb("totals", [1, 2], I32)

        ident = sb("ident", [P, P])
        ones = sb("ones", [P, P])
        zeros = sb("zeros", [P, P])
        eps = sb("eps", [P, 1])
        inv = sb("inv", [P, NB])
        has = sb("has", [P, NB])
        amp = sb("amp", [P, NB])
        att = sb("att", [P, NB])
        ids = sb("ids", [P, NB], I32)
        deg_s = sb("deg_s", [P, NB])
        start_s = sb("start_s", [P, NB])

        w0t = sb("w0t", [P, D])
        w0_bias = sb("w0_bias", [P, D])
        wt = [sb(f"wt{l}", [P, 3 * D]) for l in range(L)]
        wp = [sb(f"wp{l}", [P, T, 3, F]) for l in range(L)]
        wl = [sb(f"wl{l}", [P, D]) for l in range(L)]
        w1 = [sb(f"w1{l}", [P, DM]) for l in range(L)]
        w2 = [sb(f"w2{l}", [P, MC, D]) for l in range(L)]
        bpre = [sb(f"bpre{l}", [P, D]) for l in range(L)]
        blin = [sb(f"blin{l}", [P, D]) for l in range(L)]
        bm2 = [sb(f"bm2{l}", [P, D]) for l in range(L)]
        cols = [sb(f"cols{l}", [P, 5 + MC]) for l in range(L)]

        s_max = sb("s_max", [P, D])
        s_min = sb("s_min", [P, D])
        s_sum = sb("s_sum", [P, D])
        agg = sb("agg", [P, T, 4, F])
        aggT = sb("aggT", [P, T, P])
        sqm = sb("sqm", [P, D])
        var = sb("var", [P, D])
        scaled = sb("scaled", [P, D])
        part = sb("part", [P, D])
        o = sb("o", [P, D])
        lhs = sb("lhs", [P, D])
        x1 = sb("x1", [P, D])
        v = sb("v", [P, D])
        z1 = sb("z1", [P, D])
        z2 = sb("z2", [P, D])
        geluT = sb("geluT", [P, MC, P])
        x0b = sb("x0b", [P, D])
        st6 = sb("st6", [P, 6])
        mv = sb("mv", [P, 2])
        sd = sb("sd", [P, 1])
        rs = sb("rs", [P, 1])

        p_tr = pb("p_tr", [P, 512])
        p_lin = pb("p_lin", [P, 512])
        p_tab = pb("p_tab", [P, 512])
        p_post = pb("p_post", [P, 512])
        p_agg = pb("p_agg", [P, 512])
        p_mlp = pb("p_mlp", [P, 512])
        p_sq = pb("p_sq", [P, 512])

        off = [0, 0]

        def early(which, n, dt=F32):
            t = (A, B)[which]
            lo = off[which]
            off[which] += n
            assert off[which] <= NODEW
            v_ = t[:, lo:lo + n]
            return v_ if dt is F32 else v_.bitcast(dt)

        e_dst = early(0, EC, I32)
        e_dstf = early(0, EC)
        e_pairs = early(0, 2 * EC, I32)
        e_ends = early(0, NCH)
        e_scr = early(0, NCH)
        e_chunk = early(0, GR * CH)
        e_diag = e_chunk
        e_oh = early(1, NODEW // 2, BF16).rearrange("p (c d) -> p c d", d=P)
        e_src = B[:, 0:EC].bitcast(I32)
        e_wgt = B[:, EC:2 * EC]
        e_cum = A[:, 0:(NB + 1) * P // 2].bitcast(BF16).rearrange("p (c d) -> p c d", d=P)
        e_node = early(1, NB)
        e_node_i = early(1, NB, I32)
        e_chk = early(1, NB)
        e_chk_i = early(1, NB, I32)
        e_cnt = early(1, NB)
        e_start = early(1, NB + 1)
        e_deg = early(1, NB)
        e_clip = early(1, NB)
        e_pos = early(1, NB)
        e_pos_i = early(1, NB, I32)
        e_info = early(1, 4 * NB, I32).rearrange("p (c k) -> p c k", k=4)
        e_info_s = early(1, 4 * NB, I32).rearrange("p (c k) -> p c k", k=4)
        e_iota_i = early(1, P, I32)
        e_iota = early(1, P)
        e_onesb = early(1, P // 2, BF16)
        e_lower = early(1, P // 2, BF16)
        e_shift = early(1, P)
        e_wrap = early(1, P)
        e_tot = early(1, P)
        e_base = early(1, P)
        e_tmp = early(1, P)
        e_kk = early(1, 1)
        e_before = early(1, NB + 1)
        e_row = early(1, NB + 1)
        e_row2 = early(1, NB)
        e_rowi = early(1, NB + 1, I32)
        e_rowq = early(1, NB, I32)
        e_rowr = early(1, NB, I32)
        e_rp = early(1, 1)
        e_rp_i = early(1, 1, I32)
        e_rem = early(1, 1)
        e_run = early(1, 2 * RUN, I32)
        e_mask = early(1, RUN)
        e_si = early(1, RUN)
        e_so = early(1, RUN, I32)
        e_sa = early(1, 2 * RUN).rearrange("p (k r) -> p k r", k=2)
        e_w = early(1, 3 * D)

        edges_in = sem("edges_in")
        consts_a = sem("consts_a")
        consts = sem("consts")
        dstep = sem("dstep")
        weights_in = sem("weights_in")
        raw_in = sem("raw_in")
        wstep_pe = sem("wstep_pe")
        wstep_act = sem("wstep_act")
        dst_float = sem("dst_float")
        pairs_made = sem("pairs_made")
        dst_out = sem("dst_out")
        pairs_out = sem("pairs_out")
        tables_init = sem("tables_init")
        diag_made = sem("diag_made")
        ends_spread = sem("ends_spread")
        counted = sem("counted")
        chunk_idx = sem("chunk_idx")
        chunk_in = [sem(f"chunk_in{r}") for r in range(GR)]
        chunk_used = sem("chunk_used")
        start_made = sem("start_made")
        next_made = sem("next_made")
        onehot_made = sem("onehot_made")
        running_made = sem("running_made")
        degrees_total = sem("degrees_total")
        ranks_made = sem("ranks_made")
        ranks_used = sem("ranks_used")
        place_made = sem("place_made")
        info_out = sem("info_out")
        info_in = sem("info_in")
        sorted_made = sem("sorted_made")
        logs_made = sem("logs_made")
        deg_t = sem("deg_t")
        width_made = sem("width_made")
        begins_made = sem("begins_made")
        bounds_made = sem("bounds_made")
        x_in = sem("x_in")
        run_ready = sem("run_ready")
        run_in = sem("run_in")
        run_made = sem("run_made")
        run_out = sem("run_out")
        run_stored = sem("run_stored")
        gathered = [sem(f"gathered{r}") for r in range(RING)]
        idx_in = [sem(f"idx_in{h}") for h in range(2)]
        aux_in = [sem(f"aux_in{h}") for h in range(2)]
        slot_ready = sem("slot_ready")
        slot_used = sem("slot_used")
        squared = sem("squared")
        sq_summed = sem("sq_summed")
        hold = {k: sem(f"hold_{k}") for k in ("act", "pool", "dve")}
        table_out = sem("table_out")
        x0_out = sem("x0_out")
        x0_in = sem("x0_in")
        y_out = sem("y_out")
        cleared, summed, mean_sq, sq_free, var_done, std_ready, agg_t, agg_tc, post, amped, part_done, o_ready = (
            sem("n_" + n) for n in ("cleared", "summed", "mean_sq", "sq_free", "var_done", "std_ready", "agg_t",
                                    "agg_tc", "post", "amped", "part_done", "o_ready"))
        o_t, o_tc, lin, v1_part, v1_ready, z1_t, z1_tc, mlp1, gelued, mlp2, v2_part, v2_ready = (
            sem("n_" + n) for n in ("o_t", "o_tc", "lin", "v1_part", "v1_ready", "z1_t", "z1_tc", "mlp1", "gelued",
                                    "mlp2", "v2_part", "v2_ready"))
        stats, meanvar, sdev, rsdev, z_ready = ([sem(f"n_{n}{k}") for k in range(2)] for n in
                                                ("stats", "meanvar", "sdev", "rsdev", "z_ready"))
        z2_t, z2_tc, tab, a_part, x_part, a_ready, x_ready, b_ready = (
            sem("n_" + n) for n in ("z2_t", "z2_tc", "tab", "a_part", "x_part", "a_ready", "x_ready", "b_ready"))

        block = ctx.enter_context(nc.Block())

        def at(t, r, n=D):
            return t[:, bass.ds(r * n, n)]

        def lim(eng, e, least, most):
            return nc.s_assert_within(eng.snap(e), least, most, skip_runtime_bounds_check_because="the counts follow from the shapes")

        def val(eng, e, least=0):
            return e if isinstance(e, int) else lim(eng, e, least, 1 << 22)

        def held(eng, key, *waits):
            for s, n in waits:
                eng.wait_ge(s, n)
            eng.sem_inc(hold[key], 1)

        def quarter(eng, blk, k, n=1):
            return [eng.value_load(bounds[0:1, bass.ds(blk * 4 + j, 1)], min_val=0, max_val=SMAX - 1) for j in (k, k + n)]

        def n_slots(eng):
            return eng.value_load(totals[0:1, 0:1], min_val=2 * RING, max_val=SMAX)

        def n_turns(eng):
            return eng.value_load(totals[0:1, 1:2], min_val=2, max_val=SMAX // RING)

        @block.sync
        def _(sp):
            sp.dma_start(e_dst[0:EP, :], dst.rearrange("(p c) -> p c", p=EP)).then_inc(edges_in, 16)
            sp.dma_start(e_src[0:EP, :], src.rearrange("(p c) -> p c", p=EP)).then_inc(edges_in, 16)
            sp.dma_start(e_wgt[0:EP, :], edge_weight.rearrange("(p c) -> p c", p=EP)).then_inc(edges_in, 16)
            sp.wait_ge(dst_float, 1)
            sp.dma_start(dst_rows.rearrange("(p k) c -> p (k c)", p=EP), e_dstf[0:EP, :]).then_inc(dst_out, 16)
            sp.wait_ge(pairs_made, 1)
            sp.dma_start(pairs[0:E, :].rearrange("(p c) k -> p (c k)", p=EP), e_pairs[0:EP, :]).then_inc(pairs_out, 16)
            sp.wait_ge(consts_a, 3)
            sp.dma_start(pairs[E:E + RUN, :], zeros[0:RUN, 0:2].bitcast(I32)).then_inc(pairs_out, 16)
            sp.dma_start(tables[0][0:N, :], x).then_inc(tables_init, 16)
            sp.dma_start(tables[0][N:ZROW + 1, :], zeros[0:ZROW + 1 - N, :]).then_inc(tables_init, 16)
            for t in tables[1:]:
                sp.dma_start(t[ZROW:ZROW + 1, :], zeros[0:1, :]).then_inc(tables_init, 16)
            sp.wait_ge(info_out, 16 * NB)
            sp.dma_start(e_info_s, node_info.rearrange("(b p) k -> p b k", p=P)).then_inc(info_in, 16)
            sp.sem_inc(run_stored, 1)
            sp.wait_ge(bounds_made, 1)
            with sp.Fori(0, NB) as blk:
                lo = sp.value_load(rounds[0:1, bass.ds(blk, 1)], min_val=0, max_val=SMAX)
                hi = sp.value_load(rounds[0:1, bass.ds(blk + 1, 1)], min_val=1, max_val=SMAX)
                first = sp.value_load(bounds[0:1, bass.ds(blk * 4, 1)], min_val=0, max_val=SMAX)
                with sp.Fori(lo, hi) as q:
                    col = lim(sp, first + (q - lo) * RUN, 0, SMAX - RUN)
                    sp.wait_ge(run_made, q + 1)
                    sp.dma_start(slot_idx[:, bass.ds(col, RUN)], e_so).then_inc(run_out, 16)
                    sp.dma_start(slot_aux[:, :, bass.ds(col, RUN)], e_sa).then_inc(run_out, 16)
                    sp.wait_ge(run_out, q * 32 + 32)
                    sp.sem_inc(run_stored, 1)
            turns = n_turns(sp)
            for ps in range(3):
                k = 0 if ps == 0 else 1

                def relay(i, h):
                    turn = lim(sp, (i + turns * ps + 1) * 16, 16, 1 << 22)
                    sp.wait_ge(aux_in[h], turn)
                    for r in range(h * HALF, (h + 1) * HALF):
                        sp.wait_ge(gathered[r], turn)
                        sp.sem_inc(slot_ready, 1)

                if ps:
                    sp.wait_ge(summed, NB * ps)
                for h in range(2):
                    sp.dma_start(idx_ring[:, h * HALF:(h + 1) * HALF],
                                 slot_idx[:, h * HALF:(h + 1) * HALF]).then_inc(idx_in[h], 16)
                    a = lim(sp, ((turns * ps) % 2) * RING + h * HALF, 0, AUX - HALF) if ps else h * HALF
                    sp.dma_start(aux_ring[:, bass.ds(a, HALF)], slot_aux[:, k, h * HALF:(h + 1) * HALF]).then_inc(aux_in[h], 16)

                def refill_next(i, h):
                    c = lim(sp, i * RING + (RING + h * HALF), 0, SMAX - HALF)
                    a = lim(sp, ((i + turns * ps + 1) % 2) * RING + h * HALF, 0, AUX - HALF)
                    sp.dma_start(idx_ring[:, h * HALF:(h + 1) * HALF], slot_idx[:, bass.ds(c, HALF)]).then_inc(idx_in[h], 16)
                    sp.dma_start(aux_ring[:, bass.ds(a, HALF)], slot_aux[:, k, bass.ds(c, HALF)]).then_inc(aux_in[h], 16)

                with sp.Fori(0, turns - 1) as i:
                    for h in range(2):
                        relay(i, h)
                        refill_next(i, h)
                for h in range(2):
                    relay(turns - 1, h)
            sp.wait_ge(y_out, 16 * NB)

        @block.gpsimd
        def _(pool):
            G = nc.gpsimd
            G.memset(zeros[:, :], 0.0).then_inc(consts_a, 1)
            G.memset(ones[:, :], 1.0).then_inc(consts_a, 1)
            G.memset(eps[:, :], EPS).then_inc(consts_a, 1)
            for l in range(L):
                G.memset(wt[l][:, 0:2 * D], 0.0).then_inc(consts_a, 1)
            G.memset(e_w[:, 0:3 * D], 0.0).then_inc(consts_a, 1)
            G.iota(e_node_i, [[P, NB]], base=0, channel_multiplier=1).then_inc(consts_a, 1)
            G.iota(e_iota_i, [[1, P]], base=0, channel_multiplier=0).then_inc(consts_a, 1)
            pool.wait_ge(consts_a, 6 + L)
            for m_, src_, cmp_, fill, base, step, chan, n in (
                    (ident[:, :], zeros, ALU.not_equal, 1.0, 0, -1, 1, P),
                    (e_tmp, ones, ALU.is_ge, 0.0, -1, 1, -1, P),
                    (e_shift, zeros, ALU.not_equal, 1.0, -1, -1, 1, P),
                    (e_wrap, zeros, ALU.not_equal, 1.0, -(P - 1), 1, -P, P),
                    (e_before, ones, ALU.is_ge, 0.0, -1, 1, -1, NB + 1)):
                G.affine_select(out=m_, in_=src_[:, 0:n], compare_op=cmp_, fill=fill, base=base,
                                pattern=[[step, n]], channel_multiplier=chan).then_inc(consts, 1)
            pool.wait_ge(dst_out, 16)
            pool.wait_ge(chunk_idx, 1)
            for c in range(NB):
                r = c % GR
                if c >= GR:
                    pool.wait_ge(chunk_used, c - GR + 1)
                G.indirect_dma_start(e_chunk[:, r * CH:(r + 1) * CH], None, dst_rows,
                                     bass.IndirectOffsetOnAxis(ap=e_chk_i[:, c:c + 1], axis=0)).then_inc(chunk_in[r], 16)
            pool.wait_ge(place_made, 1)
            for c in range(NB):
                G.indirect_dma_start(node_info, bass.IndirectOffsetOnAxis(ap=e_pos_i[:, c:c + 1], axis=0),
                                     e_info[:, c, :], None).then_inc(info_out, 16)
            pool.wait_ge(pairs_out, 32)
            pool.wait_ge(bounds_made, 1)
            n_fetch = pool.value_load(rounds[0:1, NB:NB + 1], min_val=1, max_val=SMAX)
            with pool.Fori(0, n_fetch) as q:
                held(pool, "pool", (run_ready, q + 1))
                G.indirect_dma_start(e_run, None, pairs_e,
                                     bass.IndirectOffsetOnAxis(ap=e_rp_i, axis=0)).then_inc(run_in, 16)
            pool.wait_ge(tables_init, 16 * (2 + L))
            pool.wait_ge(sorted_made, 1)
            for blk in range(NB):
                G.indirect_dma_start(X[:, blk * D:(blk + 1) * D], None, tables[0],
                                     bass.IndirectOffsetOnAxis(ap=ids[:, blk:blk + 1], axis=0)).then_inc(x_in, 16)
            turns = n_turns(pool)
            for ps in range(3):
                with pool.Fori(0, turns) as i:
                    turn = lim(pool, (i + turns * ps + 1) * 16, 16, 1 << 22)
                    g = lim(pool, (i + turns * ps) * RING, 0, 1 << 22)
                    g1 = lim(pool, (i + turns * (ps - 1)) * RING, 0, 1 << 22) if ps else 0
                    for r in range(RING):
                        if r % HALF == 0:
                            pool.wait_ge(idx_in[r // HALF], turn)
                        if r % QRT == 0:
                            pool.wait_ge(slot_used, g + (r + QRT))
                            if ps:
                                pool.wait_ge(squared, g1 + (r + QRT))
                            pool.sem_inc(hold["pool"], 1)
                        G.indirect_dma_start(ring[:, r * D:(r + 1) * D], None, tables[ps],
                                             bass.IndirectOffsetOnAxis(ap=idx_ring[:, r:r + 1], axis=0)).then_inc(gathered[r], 16)
                for blk in range(NB):
                    if ps < 2:
                        pool.wait_ge(b_ready, NB * ps + blk + 1)
                        G.indirect_dma_start(tables[ps + 1], bass.IndirectOffsetOnAxis(ap=ids[:, blk:blk + 1], axis=0),
                                             B[:, blk * D:(blk + 1) * D], None).then_inc(table_out, 16)
                    else:
                        n = P if blk < NB - 1 else LAST
                        pool.wait_ge(z_ready[1], NB * ps + blk + 1)
                        G.indirect_dma_start(out, bass.IndirectOffsetOnAxis(ap=ids[0:n, blk:blk + 1], axis=0),
                                             B[0:n, blk * D:(blk + 1) * D], None).then_inc(y_out, 16)
                if ps < 2:
                    pool.wait_ge(table_out, 16 * NB * (ps + 1))
            pool.wait_ge(y_out, 16 * NB)

        @block.vector
        def _(dve):
            V = nc.vector
            cnt = [0]

            def link(ins):
                cnt[0] += 1
                ins.then_inc(dstep, 1)
                dve.wait_ge(dstep, cnt[0])

            dve.sem_inc(slot_used, RING)
            dve.sem_inc(sq_free, 1)
            dve.wait_ge(edges_in, 48)
            V.tensor_copy(e_dstf[0:EP, :], e_dst[0:EP, :]).then_inc(dst_float, 1)
            pv = e_pairs[0:EP, :].rearrange("p (c k) -> p c k", k=2)
            link(V.tensor_copy(pv[:, :, 0], e_src[0:EP, :]))
            V.tensor_copy(pv[:, :, 1].bitcast(F32), e_wgt[0:EP, :]).then_inc(pairs_made, 1)
            dve.wait_ge(consts, 5)
            dve.wait_ge(dst_float, 1)
            for j in range(CPP):
                V.tensor_scalar(e_diag[0:EP, j * P:j * P + EP], ident[0:EP, 0:EP],
                                e_dstf[0:EP, (j + 1) * CH - 1:(j + 1) * CH], None, ALU.mult).then_inc(diag_made, 1)
            link(V.tensor_copy(e_node, e_node_i))
            dve.wait_ge(ends_spread, 1)
            link(V.tensor_copy(e_ends, p_post[:, 0:NCH]))
            with dve.Fori(0, NB) as c:
                V.tensor_scalar(e_scr, e_ends, e_node[:, bass.ds(c, 1)], 0.0, ALU.is_lt, ALU.add,
                                accum_out=e_chk[:, bass.ds(c, 1)]).then_inc(counted, 1)
                dve.wait_ge(counted, c + 1)
            link(V.tensor_scalar(e_chk, e_chk, float(NCH - 1), None, ALU.min))
            V.tensor_copy(e_chk_i, e_chk).then_inc(chunk_idx, 1)
            for c in range(NB):
                r = c % GR
                dve.wait_ge(chunk_in[r], 16 * (c // GR + 1))
                V.tensor_scalar(e_chunk[:, r * CH:(r + 1) * CH], e_chunk[:, r * CH:(r + 1) * CH], e_node[:, c:c + 1], 0.0,
                                ALU.is_lt, ALU.add, accum_out=e_cnt[:, c:c + 1]).then_inc(chunk_used, 1)
            dve.wait_ge(chunk_used, NB)
            link(V.scalar_tensor_tensor(e_start[:, 0:NB], e_chk, float(CH), e_cnt, ALU.mult, ALU.add))
            link(V.memset(e_start[:, NB:NB + 1], float(E)))
            V.tensor_copy(e_info[:, :, 0], e_start[:, 0:NB]).then_inc(start_made, 1)
            dve.wait_ge(next_made, 1)
            link(V.scalar_tensor_tensor(e_deg, e_start[:, 0:NB], -1.0, p_post[:, 0:NB], ALU.mult, ALU.add))
            link(V.tensor_scalar(e_clip, e_deg, float(P - 1), None, ALU.min))
            link(V.tensor_copy(e_info[:, :, 1], e_deg))
            link(V.tensor_copy(e_info[:, :, 2], e_node))
            link(V.tensor_copy(e_info[:, :, 3], e_node))
            link(V.tensor_copy(e_iota, e_iota_i))
            link(V.tensor_copy(e_onesb, ones[:, :]))
            link(V.tensor_copy(e_lower, e_tmp))
            V.tensor_tensor(e_oh, e_iota.unsqueeze(1).to_broadcast([P, NB, P]),
                            e_clip.unsqueeze(2).to_broadcast([P, NB, P]), ALU.is_equal).then_inc(onehot_made, 1)
            dve.wait_ge(dst_out, 16)
            dve.wait_ge(pairs_out, 32)
            V.memset(e_cum[:, 0, :], 0.0).then_inc(running_made, 1)
            dve.wait_ge(onehot_made, 1)
            with dve.Fori(0, NB) as c:
                dve.wait_ge(running_made, c + 1)
                V.tensor_tensor(e_cum[:, bass.ds(c + 1, 1), :], e_cum[:, bass.ds(c, 1), :], e_oh[:, bass.ds(c, 1), :],
                                ALU.add).then_inc(running_made, 1)
            dve.wait_ge(degrees_total, 1)
            link(V.tensor_tensor_scan(e_tot, ones[:, :], p_agg[:, 0:P], 0.0, ALU.mult, ALU.add))
            link(V.tensor_scalar(e_base, e_tot, -1.0, float(NP), ALU.mult, ALU.add))
            scr = e_scr[:, 0:2 * P].rearrange("p (c d) -> p c d", d=P)
            base1 = cnt[0]
            with dve.Fori(0, NB // 2) as c:
                dve.wait_ge(ranks_made, c + 1)
                V.tensor_tensor(scr, p_post[:, 0:2 * P].rearrange("p (c d) -> p c d", d=P),
                                e_base.unsqueeze(1).to_broadcast([P, 2, P]), ALU.add).then_inc(dstep, 1)
                dve.wait_ge(dstep, c * 2 + (base1 + 1))
                V.tensor_tensor(scr, scr, e_oh[:, bass.ds(c * 2, 2), :], ALU.mult).then_inc(dstep, 1)
                dve.wait_ge(dstep, c * 2 + (base1 + 2))
                V.tensor_reduce(e_pos[:, bass.ds(c * 2, 2)], scr, AX.X, ALU.add).then_inc(ranks_used, 1)
                dve.wait_ge(ranks_used, c + 1)
            cnt[0] += NB
            V.tensor_copy(e_pos_i, e_pos).then_inc(place_made, 1)
            dve.wait_ge(info_in, 16)
            link(V.tensor_copy(start_s[:, :], e_info_s[:, :, 0]))
            link(V.tensor_copy(ids[:, :], e_info_s[:, :, 2]))
            V.tensor_copy(deg_s[:, :], e_info_s[:, :, 1]).then_inc(sorted_made, 1)
            dve.wait_ge(sorted_made, 1)
            link(V.tensor_scalar(inv[:, :], deg_s[:, :], 1.0, None, ALU.max))
            link(V.tensor_scalar(att[:, :], inv[:, :], 1.0, None, ALU.add))
            link(V.tensor_scalar(has[:, :], deg_s[:, :], 1.0, None, ALU.min))
            V.reciprocal(inv[:, :], inv[:, :]).then_inc(sorted_made, 1)
            dve.wait_ge(logs_made, 1)
            link(V.reciprocal(att[:, :], amp[:, :]))
            link(V.tensor_scalar(att[:, :], att[:, :], AVG_LOG, None, ALU.mult))
            link(V.tensor_scalar(amp[:, :], amp[:, :], 1.0 / AVG_LOG, None, ALU.mult))
            dve.wait_ge(deg_t, 1)
            link(V.tensor_reduce(e_kk[0:NB, :], p_lin[0:NB, 0:P], AX.X, ALU.max))
            V.tensor_scalar(e_kk[0:NB, :], e_kk[0:NB, :], 4.0, None, ALU.max).then_inc(width_made, 1)
            dve.wait_ge(begins_made, 1)
            link(V.tensor_copy(e_row[0:1, :], p_lin[0:1, 0:NB + 1]))
            link(V.tensor_scalar(e_row[0:1, NB:NB + 1], e_row[0:1, NB:NB + 1], float(RING - 1), None, ALU.add))
            link(V.tensor_copy(e_rowi[0:1, :], e_row[0:1, :]))
            endc = e_rowi[0:1, NB:NB + 1]
            link(V.tensor_scalar(totals[0:1, 1:2], endc, 5, None, ALU.logical_shift_right))
            link(V.tensor_scalar(totals[0:1, 0:1], totals[0:1, 1:2], 5, None, ALU.logical_shift_left))
            link(V.tensor_copy(endc, totals[0:1, 0:1]))
            link(V.tensor_copy(e_row[0:1, :], e_rowi[0:1, :]))
            link(V.tensor_tensor(e_row2[0:1, :], e_row[0:1, 1:NB + 1], e_row[0:1, 0:NB], ALU.subtract))
            link(V.tensor_copy(e_rowq[0:1, :], e_row2[0:1, :]))
            link(V.tensor_scalar(e_rowr[0:1, :], e_rowq[0:1, :], 2, None, ALU.logical_shift_right))
            bq = bounds[0:1, 0:4 * NB].rearrange("p (b k) -> p b k", k=4)
            link(V.tensor_copy(bq[:, :, 0], e_rowi[0:1, 0:NB]))
            link(V.tensor_copy(bounds[0:1, 4 * NB:4 * NB + 1], endc))
            for k in range(3):
                link(V.tensor_tensor(bq[:, :, k + 1], bq[:, :, k], e_rowr[0:1, :], ALU.add))
            link(V.tensor_scalar(e_row2[0:1, :], e_row2[0:1, :], float(RUN - 1), None, ALU.add))
            link(V.tensor_copy(e_rowq[0:1, :], e_row2[0:1, :]))
            link(V.tensor_scalar(e_rowr[0:1, :], e_rowq[0:1, :], RUN.bit_length() - 1, None, ALU.logical_shift_right))
            link(V.tensor_copy(e_row2[0:1, :], e_rowr[0:1, :]))
            link(V.memset(e_row[0:1, 0:1], 0.0))
            link(V.tensor_tensor_scan(e_row[0:1, 1:NB + 1], ones[0:1, 0:NB], e_row2[0:1, :], 0.0, ALU.mult, ALU.add))
            V.tensor_copy(rounds[0:1, :], e_row[0:1, :]).then_inc(bounds_made, 1)
            dve.wait_ge(bounds_made, 1)

            base2 = cnt[0]
            pair = e_run.rearrange("p (r k) -> p r k", k=2)
            with dve.Fori(0, NB) as blk:
                lo = dve.value_load(rounds[0:1, bass.ds(blk, 1)], min_val=0, max_val=SMAX)
                hi = dve.value_load(rounds[0:1, bass.ds(blk + 1, 1)], min_val=1, max_val=SMAX)
                V.tensor_copy(e_rp, start_s[:, bass.ds(blk, 1)]).then_inc(dstep, 1)
                V.tensor_copy(e_rem, deg_s[:, bass.ds(blk, 1)]).then_inc(dstep, 1)
                with dve.Fori(lo, hi) as q:
                    t = lim(dve, q * 7 + blk * 2 + (base2 + 2), 0, 1 << 22)
                    dve.wait_ge(dstep, t)
                    V.tensor_scalar(e_rp_i, e_rp, 2.0, None, ALU.mult).then_inc(run_ready, 1)
                    V.tensor_scalar(e_mask, e_iota[:, 0:RUN], e_rem, None, ALU.is_lt).then_inc(dstep, 1)
                    dve.wait_ge(run_ready, q + 1)
                    V.tensor_scalar(e_rp, e_rp, float(RUN), float(E), ALU.add, ALU.min).then_inc(dstep, 1)
                    dve.wait_ge(dstep, t + 2)
                    V.tensor_scalar(e_rem, e_rem, -float(RUN), None, ALU.add).then_inc(dstep, 1)
                    dve.wait_ge(run_in, q * 16 + 16)
                    V.scalar_tensor_tensor(e_si, pair[:, :, 0], -float(ZROW), e_mask, ALU.add, ALU.mult).then_inc(dstep, 1)
                    dve.wait_ge(dstep, t + 4)
                    dve.wait_ge(run_stored, q + 1)
                    V.tensor_scalar(e_so, e_si, float(ZROW), None, ALU.add).then_inc(dstep, 1)
                    V.tensor_tensor(e_sa[:, 0, :], pair[:, :, 1].bitcast(F32), e_mask, ALU.mult).then_inc(dstep, 1)
                    V.tensor_scalar(e_sa[:, 1, :], e_mask, -BIG, BIG, ALU.mult, ALU.add).then_inc(dstep, 1)
                    dve.wait_ge(dstep, t + 7)
                    dve.sem_inc(run_made, 1)

            slots_n = n_slots(dve)

            def normalise(k, turn, src_, dst_):
                V.bn_stats(st6[:, :], src_).then_inc(stats[k], 1)
                held(dve, "dve", (stats[k], turn))
                V.bn_aggr(mv[:, :], st6[:, :]).then_inc(meanvar[k], 1)
                dve.wait_ge(sdev[k], turn)
                V.reciprocal(rs[:, :], sd[:, :]).then_inc(rsdev[k], 1)
                dve.wait_ge(rsdev[k], turn)
                V.tensor_scalar(dst_, src_, mv[:, 0:1], rs[:, :], ALU.subtract, ALU.mult).then_inc(z_ready[k], 1)
                held(dve, "dve", (z_ready[k], turn))

            def table_stage(l, blk, turn, state):
                dve.wait_ge(tab, turn)
                V.tensor_tensor(at(A, blk), p_tab[:, 0:D], bpre[l][:, :], ALU.add).then_inc(a_part, 1)
                V.tensor_tensor(at(X, blk), state, p_tab[:, 2 * D:3 * D], ALU.add).then_inc(x_part, 1)
                dve.wait_ge(a_part, turn)
                V.tensor_scalar(at(A, blk), at(A, blk), has[:, bass.ds(blk, 1)], None, ALU.mult).then_inc(a_ready, 1)
                dve.wait_ge(x_part, turn)
                V.tensor_tensor(at(X, blk), at(X, blk), blin[l][:, :], ALU.add).then_inc(x_ready, 1)
                held(dve, "dve", (x_ready, turn))

            dve.wait_ge(weights_in, W_IN)
            dve.wait_ge(x_in, 16 * NB)
            with dve.Fori(0, NB) as blk:
                turn = val(dve, blk + 1, 1)
                lo, hi = quarter(dve, blk, 0, 4)
                V.memset(s_sum[:, :], 0.0).then_inc(cleared, 1)
                held(dve, "dve", (cleared, turn))
                with dve.Fori(lo, hi) as g:
                    dve.wait_ge(slot_ready, g + 1)
                    dve.wait_ge(slot_used, g + RING)
                    V.scalar_tensor_tensor(s_sum[:, :], at(ring, g % RING), aux_ring[:, bass.ds(g % AUX, 1)], s_sum[:, :],
                                           ALU.mult, ALU.add).then_inc(slot_used, 1)
                dve.wait_ge(slot_used, hi + RING)
                V.tensor_copy(o[:, :], s_sum[:, :]).then_inc(summed, 1)
                dve.wait_ge(lin, turn)
                V.tensor_tensor(v[:, :], p_lin[:, 0:D], at(X, blk), ALU.add).then_inc(v1_part, 1)
                dve.wait_ge(v1_part, turn)
                V.tensor_tensor(v[:, :], v[:, :], w0_bias[:, :], ALU.add).then_inc(v1_ready, 1)
                dve.wait_ge(v1_ready, turn)
                normalise(0, turn, v[:, :], z1[:, :])
                normalise(1, turn, z1[:, :], z2[:, :])
                table_stage(0, blk, turn, z1[:, :])
                held(dve, "dve", (x0_out, turn * 16))

            for ps in (1, 2):
                def clear(blk):
                    V.memset(s_sum[:, :], 0.0).then_inc(cleared, 1)
                    V.memset(s_max[:, :], -BIG).then_inc(cleared, 1)
                    V.memset(s_min[:, :], BIG).then_inc(cleared, 1)
                    held(dve, "dve", (cleared, val(dve, blk * 3 + (NB + 3 * NB * (ps - 1) + 3), 1)))

                def slots(blk, k):
                    lo, hi = quarter(dve, blk, k)
                    lo2 = lim(dve, lo + slots_n * ps, 0, 1 << 22)
                    hi2 = lim(dve, hi + slots_n * ps, 1, 1 << 22)
                    with dve.Fori(lo2, hi2) as g:
                        row = lim(dve, (g % RING) * D, 0, (RING - 1) * D)
                        aux = lim(dve, g % AUX, 0, AUX - 1)
                        rows = ring[:, bass.ds(row, D)]
                        guard = aux_ring[:, bass.ds(aux, 1)]
                        dve.wait_ge(slot_ready, g + 1)
                        dve.wait_ge(slot_used, g + RING)
                        V.scalar_tensor_tensor(s_max[:, :], rows, guard, s_max[:, :], ALU.subtract, ALU.max)
                        V.scalar_tensor_tensor(s_min[:, :], rows, guard, s_min[:, :], ALU.add, ALU.min)
                        V.tensor_tensor(s_sum[:, :], rows, s_sum[:, :], ALU.add).then_inc(slot_used, 1)

                def tiles(t):
                    return t.rearrange("p (t f) -> p t f", f=F)

                def aggregates(blk):
                    turn = val(dve, blk + (1 + NB * ps), 1)
                    turn1 = val(dve, blk + (1 + NB * (ps - 1)), 1)
                    end = dve.value_load(bounds[0:1, bass.ds(blk * 4 + 4, 1)], min_val=1, max_val=SMAX)
                    dve.wait_ge(slot_used, end + slots_n * ps + RING)
                    h1, a_ = has[:, bass.ds(blk, 1)], tiles(at(A, blk))
                    V.scalar_tensor_tensor(agg[:, :, 0, :], tiles(s_sum[:, :]), inv[:, bass.ds(blk, 1)], a_,
                                           ALU.mult, ALU.add).then_inc(summed, 1)
                    V.scalar_tensor_tensor(agg[:, :, 1, :], tiles(s_min[:, :]), h1, a_, ALU.mult, ALU.add)
                    V.scalar_tensor_tensor(agg[:, :, 2, :], tiles(s_max[:, :]), h1, a_, ALU.mult, ALU.add)
                    dve.wait_ge(mean_sq, turn1)
                    dve.wait_ge(sq_summed, end + slots_n * (ps - 1) + SQR)
                    V.scalar_tensor_tensor(var[:, :], p_sq[:, 0:D], inv[:, bass.ds(blk, 1)], sqm[:, :],
                                           ALU.mult, ALU.subtract).then_inc(sq_free, 1)
                    dve.wait_ge(sq_free, turn1 + 1)
                    V.tensor_scalar(var[:, :], var[:, :], 0.0, EPS, ALU.max, ALU.add).then_inc(var_done, 1)
                    held(dve, "dve", (var_done, turn1))

                def combine(blk):
                    turn1 = val(dve, blk + (1 + NB * (ps - 1)), 1)
                    pp = p_post[:, 0:3 * D].rearrange("p (t s f) -> p t s f", t=T, s=3)
                    dve.wait_ge(amped, turn1)
                    V.scalar_tensor_tensor(tiles(part[:, :]), pp[:, :, 2, :], att[:, bass.ds(blk, 1)], tiles(scaled[:, :]),
                                           ALU.mult, ALU.add).then_inc(part_done, 1)
                    dve.wait_ge(part_done, turn1)
                    V.tensor_tensor(tiles(o[:, :]), pp[:, :, 0, :], tiles(part[:, :]), ALU.add).then_inc(o_ready, 1)

                def after_conv(blk):
                    turn = val(dve, blk + (1 + NB * ps), 1)
                    dve.wait_ge(lin, turn)
                    V.tensor_tensor(x1[:, :], p_lin[:, 0:D], at(X, blk), ALU.add).then_inc(v1_ready, 1)
                    dve.wait_ge(v1_ready, turn)
                    normalise(0, turn, x1[:, :], z1[:, :])

                def after_mlp(blk):
                    turn = val(dve, blk + (1 + NB * ps), 1)
                    turn1 = val(dve, blk + (1 + NB * (ps - 1)), 1)
                    dve.wait_ge(mlp2, turn1)
                    V.tensor_tensor(v[:, :], p_lin[:, 0:D], x1[:, :], ALU.add).then_inc(v2_part, 1)
                    dve.wait_ge(v2_part, val(dve, blk * ps + (1 + NB * (ps - 1)), 1))
                    if ps == 2:
                        dve.wait_ge(x0_in, val(dve, blk * 16 + 16, 1))
                        V.tensor_tensor(v[:, :], v[:, :], x0b[:, :], ALU.add).then_inc(v2_part, 1)
                        dve.wait_ge(v2_part, val(dve, blk * ps + (2 + NB * (ps - 1)), 1))
                    V.tensor_tensor(v[:, :], v[:, :], bm2[ps - 1][:, :], ALU.add).then_inc(v2_ready, 1)
                    dve.wait_ge(v2_ready, turn1)
                    normalise(1, turn, v[:, :], z2[:, :] if ps == 1 else at(B, blk))

                def finish(blk):
                    if ps == 1:
                        table_stage(1, blk, val(dve, blk + (1 + NB * ps), 1), v[:, :])

                if ps == 2:
                    dve.wait_ge(table_out, 16 * NB * 2)
                clear(0)
                for k in range(4):
                    slots(0, k)
                aggregates(0)
                with dve.Fori(1, NB) as blk:
                    clear(blk)
                    for k, tail in enumerate((combine, after_conv, after_mlp, finish)):
                        slots(blk, k)
                        tail(blk - 1)
                    aggregates(blk)
                for tail in (combine, after_conv, after_mlp, finish):
                    tail(NB - 1)

        @block.scalar
        def _(act):
            C = nc.scalar
            act.sem_inc(squared, RING)
            n_w = [0, 0]

            def load(dst_, src_):
                act.dma_start(dst_, src_).then_inc(weights_in, 16)
                n_w[0] += 1

            def row(v_):
                return v_.unsqueeze(0).to_broadcast([P, D])

            def col(v_):
                return v_.rearrange("(p o) -> p o", o=1)

            act.wait_ge(consts_a, 6 + L)
            act.dma_start(e_w[:, 0:D], W).then_inc(raw_in, 16)
            for l in range(L):
                for t in range(T):
                    d0 = e_w[t * F:(t + 1) * F, (l + 1) * D + t * F:(l + 1) * D + (t + 1) * F]
                    act.dma_start(d0, W_post[l, t, 0:F, :]).then_inc(raw_in, 16)
            load(w0_bias[:, :], row(b))
            for l in range(L):
                load(wl[l][:, :], W_lin[l])
                load(w1[l][:, :], W1[l])
                load(w2[l][:, :, :], W2[l].rearrange("(c p) g -> p c g", p=P))
                load(bpre[l][:, :], row(b_pre[l].rearrange("t f -> (t f)")))
                load(blin[l][:, :], row(b_lin[l]))
                load(bm2[l][:, :], row(b2[l]))
                for k, v_ in enumerate((ln1_g[l], ln1_b[l], ln2_g[l], ln2_b[l], b_post[l].rearrange("t f -> (t f)"))):
                    load(cols[l][:, k:k + 1], col(v_))
                for c in range(MC):
                    load(cols[l][:, 5 + c:6 + c], col(b1[l, c * P:(c + 1) * P]))
                for t in range(T):
                    load(wt[l][t * F:(t + 1) * F, t * F:(t + 1) * F], W_pre[l, t, 0:F, :])
                    load(wt[l][t * F:(t + 1) * F, D + t * F:D + (t + 1) * F], W_pre[l, t, F:2 * F, :])
                    load(wp[l][:, t, :, :], W_post[l, t, F:13 * F, :].rearrange("(s p) g -> p s g", p=P))
            assert 16 * n_w[0] == W_IN
            act.wait_ge(weights_in, W_IN)
            n_s = 0
            act.wait_ge(wstep_pe, 1)
            C.copy(w0t[:, :], p_tr[:, 0:D]).then_inc(wstep_act, 1)
            for l in range(L):
                C.activation(x1[:, :], ones[:, :], ACT.Identity, scale=cols[l][:, 4:5]).then_inc(wstep_act, 1)
                act.wait_ge(wstep_pe, 2 + 3 * l)
                C.copy(lhs[:, :], p_tr[:, 0:D]).then_inc(wstep_act, 1)
                act.wait_ge(wstep_pe, 3 + 3 * l)
                C.copy(wt[l][:, 2 * D:3 * D], p_tab[:, 0:D]).then_inc(wstep_act, 1)
                act.wait_ge(wstep_pe, 4 + 3 * l)
                C.copy(blin[l][:, :], p_mlp[:, 0:D]).then_inc(wstep_act, 1)
            act.wait_ge(sorted_made, 2)
            C.activation(amp[:, :], att[:, :], ACT.Ln).then_inc(logs_made, 1)
            act.wait_ge(bounds_made, 1)
            slots_n = n_slots(act)

            def root(k, turn):
                held(act, "act", (meanvar[k], turn))
                C.activation(sd[:, :], mv[:, 1:2], ACT.Sqrt, bias=eps[:, :]).then_inc(sdev[k], 1)

            def affine(l, k, turn, arrived, done):
                held(act, "act", (arrived, turn))
                C.activation(lhs[:, :], p_tr[:, 0:D], ACT.Identity, bias=cols[l][:, k + 1:k + 2],
                             scale=cols[l][:, k:k + 1]).then_inc(done, 1)

            def keep_rows(blk, turn):
                held(act, "act", (x_part, turn))
                C.copy(at(B, blk), p_tab[:, D:2 * D]).then_inc(b_ready, 1)

            with act.Fori(0, NB) as blk:
                turn = val(act, blk + 1, 1)
                held(act, "act", (o_t, turn))
                C.copy(lhs[:, :], p_tr[:, 0:D]).then_inc(o_tc, 1)
                root(0, turn)
                held(act, "act", (z_ready[0], turn))
                act.dma_start(x0_rows[bass.ds(blk, 1), :, :].rearrange("a p d -> (a p) d"), z1[:, :]).then_inc(x0_out, 16)
                root(1, turn)
                affine(0, 0, turn, z2_t, z2_tc)
                keep_rows(blk, turn)

            for ps in (1, 2):
                def slots(blk, k):
                    lo, hi = quarter(act, blk, k)
                    lo2 = lim(act, lo + slots_n * (ps - 1), 0, 1 << 22)
                    hi2 = lim(act, hi + slots_n * (ps - 1), 1, 1 << 22)
                    with act.Fori(lo2, hi2) as g:
                        held(act, "act", (slot_ready, g + slots_n + 1), (sq_summed, g + 1))
                        C.activation(at(sq_ring, g % SQR), at(ring, g % RING), ACT.Square).then_inc(squared, 1)

                def aggregates(blk):
                    turn = val(act, blk + (1 + NB * ps), 1)
                    turn1 = val(act, blk + (1 + NB * (ps - 1)), 1)
                    held(act, "act", (summed, turn))
                    C.activation(sqm[:, :], s_sum[:, :], ACT.Square, scale=inv[:, bass.ds(blk, 1)]).then_inc(mean_sq, 1)
                    held(act, "act", (var_done, turn1))
                    C.activation(agg[:, :, 3, :], var[:, :].rearrange("p (t f) -> p t f", f=F), ACT.Sqrt).then_inc(std_ready, 1)
                    held(act, "act", (agg_t, turn1))
                    C.copy(aggT[:, :, :], p_agg[:, :].rearrange("p (t n) -> p t n", n=P)).then_inc(agg_tc, 1)
                    held(act, "act", (post, turn1))
                    C.activation(scaled[:, :].rearrange("p (t f) -> p t f", f=F),
                                 p_post[:, 0:3 * D].rearrange("p (t s f) -> p t s f", t=T, s=3)[:, :, 1, :],
                                 ACT.Copy, scale=amp[:, bass.ds(blk, 1)]).then_inc(amped, 1)

                def transposed(blk):
                    held(act, "act", (o_t, val(act, blk + (1 + NB * ps), 1)))
                    C.copy(lhs[:, :], p_tr[:, 0:D]).then_inc(o_tc, 1)

                def mlp(blk):
                    turn = val(act, blk + (1 + NB * ps), 1)
                    turn1 = val(act, blk + (1 + NB * (ps - 1)), 1)
                    root(0, turn)
                    affine(ps - 1, 2, turn1, z1_t, z1_tc)
                    held(act, "act", (mlp1, turn1))
                    for c in range(MC):
                        C.activation(geluT[:, c, :], p_mlp[:, c * P:(c + 1) * P], ACT.Gelu,
                                     bias=cols[ps - 1][:, 5 + c:6 + c]).then_inc(gelued, 1)
                    if ps == 2:
                        act.dma_start(x0b[:, :], x0_rows[bass.ds(blk, 1), :, :].rearrange("a p d -> (a p) d")).then_inc(x0_in, 16)

                def after_mlp(blk):
                    turn = val(act, blk + (1 + NB * ps), 1)
                    root(1, turn)
                    if ps == 1:
                        affine(1, 0, turn, z2_t, z2_tc)

                def finish(blk):
                    if ps == 1:
                        keep_rows(blk, val(act, blk + (1 + NB * ps), 1))

                if ps == 1:
                    act.wait_ge(table_out, 16 * NB)
                    act.wait_ge(x0_out, 16 * NB)
                for k in range(4):
                    slots(0, k)
                aggregates(0)
                with act.Fori(1, NB) as blk:
                    for k, tail in enumerate((transposed, mlp, after_mlp, finish)):
                        slots(blk, k)
                        tail(blk - 1)
                    aggregates(blk)
                for tail in (transposed, mlp, after_mlp, finish):
                    tail(NB - 1)

        @block.tensor
        def _(pe):
            M = nc.tensor
            pe.sem_inc(sq_summed, SQR)
            pe.wait_ge(consts, 5)
            pe.wait_ge(diag_made, CPP)
            for j in range(CPP):
                last = M.matmul(p_post[:, j * EP:(j + 1) * EP], ones[0:EP, :], e_diag[0:EP, j * P:j * P + EP], start=True, stop=True)
            last.then_inc(ends_spread, 1)
            pe.wait_ge(raw_in, 16 * (1 + L * T))
            M.transpose(p_tr[:, 0:D], e_w[:, 0:D], ident[:, :]).then_inc(wstep_pe, 1)
            pe.wait_ge(weights_in, W_IN)
            for l in range(L):
                pe.wait_ge(wstep_act, 1 + 4 * l)
                M.transpose(p_tr[:, 0:D], e_w[:, (l + 1) * D:(l + 2) * D], ident[:, :]).then_inc(wstep_pe, 1)
                pe.wait_ge(wstep_act, 3 + 4 * l)
                M.matmul(p_tab[:, 0:D], lhs[:, :], wl[l][:, :], start=True, stop=True).then_inc(wstep_pe, 1)
                M.matmul(p_mlp[:, 0:D], x1[:, :], wl[l][:, :], start=True, stop=False)
                M.matmul(p_mlp[:, 0:D], ident[:, :], blin[l][:, :], start=False, stop=True).then_inc(wstep_pe, 1)
            pe.wait_ge(start_made, 1)
            M.matmul(p_post[:, 0:NB], e_shift, e_start[:, 0:NB], start=True, stop=False)
            M.matmul(p_post[:, 0:NB], e_wrap, e_start[:, 1:NB + 1], start=False, stop=True).then_inc(next_made, 1)
            pe.wait_ge(running_made, NB + 1)
            M.matmul(p_agg[:, 0:P], e_onesb, e_cum[:, NB, :], start=True, stop=True).then_inc(degrees_total, 1)

            def ranks(c):
                two = p_post[:, 0:2 * P].rearrange("p (c d) -> p c d", d=P)
                M.matmul(two, e_lower, e_oh[:, bass.ds(c * 2, 2), :], start=True, stop=False)
                M.matmul(two, e_onesb, e_cum[:, bass.ds(c * 2, 2), :], start=False, stop=True).then_inc(ranks_made, 1)

            ranks(0)
            with pe.Fori(1, NB // 2) as c:
                pe.wait_ge(ranks_used, c)
                ranks(c)
            pe.wait_ge(sorted_made, 1)
            M.transpose(p_lin[0:NB, 0:P], deg_s[:, :], ident[:, :]).then_inc(deg_t, 1)
            pe.wait_ge(width_made, 1)
            M.matmul(p_lin[0:1, 0:NB + 1], e_kk[0:NB, :], e_before[0:NB, :], start=True, stop=True).then_inc(begins_made, 1)

            pe.wait_ge(bounds_made, 1)
            pe.wait_ge(wstep_act, 1 + 4 * L)
            slots_n = n_slots(pe)

            def linear(w, turn):
                M.transpose(p_tr[:, 0:D], o[:, :], ident[:, :]).then_inc(o_t, 1)
                pe.wait_ge(o_tc, turn)
                M.matmul(p_lin[:, 0:D], lhs[:, :], w, start=True, stop=True).then_inc(lin, 1)

            def table_stage(l, turn):
                pe.wait_ge(z_ready[1], turn)
                M.transpose(p_tr[:, 0:D], z2[:, :], ident[:, :]).then_inc(z2_t, 1)
                pe.wait_ge(z2_tc, turn)
                M.matmul(p_tab[:, 0:3 * D], lhs[:, :], wt[l][:, :], start=True, stop=True).then_inc(tab, 1)

            with pe.Fori(0, NB) as blk:
                turn = val(pe, blk + 1, 1)
                pe.wait_ge(summed, turn)
                linear(w0t[:, :], turn)
                table_stage(0, turn)

            for ps in (1, 2):
                def slots(blk, k):
                    lo, hi = quarter(pe, blk, k)
                    lo2 = lim(pe, lo + slots_n * (ps - 1), 0, 1 << 22)
                    hi2 = lim(pe, hi + slots_n * (ps - 1), 1, 1 << 22)
                    if k == 0:
                        pe.wait_ge(sq_free, val(pe, blk + (1 + NB * (ps - 1)), 1))
                        M.matmul(p_sq[:, 0:D], ident[:, :], zeros[:, :], start=True, stop=True)
                    with pe.Fori(lo2, hi2) as g:
                        pe.wait_ge(squared, g + (RING + 1))
                        M.matmul(p_sq[:, 0:D], ident[:, :], at(sq_ring, g % SQR), start=False, stop=True,
                                 skip_group_check=True).then_inc(sq_summed, 1)

                def aggregates(blk):
                    turn1 = val(pe, blk + (1 + NB * (ps - 1)), 1)
                    pe.wait_ge(std_ready, turn1)
                    for t in range(T):
                        last = M.transpose(p_agg[:, t * P:(t + 1) * P], agg[:, t, :, :].rearrange("p a f -> p (a f)"), ident[:, :])
                    last.then_inc(agg_t, 1)
                    pe.wait_ge(agg_tc, turn1)
                    for t in range(T):
                        last = M.matmul(p_post[:, t * 3 * F:(t + 1) * 3 * F], aggT[:, t, :],
                                        wp[ps - 1][:, t, :, :].rearrange("p s g -> p (s g)"), start=True, stop=True)
                    last.then_inc(post, 1)

                def transposed(blk):
                    pe.wait_ge(o_ready, val(pe, blk + (1 + NB * (ps - 1)), 1))
                    linear(wl[ps - 1][:, :], val(pe, blk + (1 + NB * ps), 1))

                def mlp(blk):
                    turn1 = val(pe, blk + (1 + NB * (ps - 1)), 1)
                    pe.wait_ge(z_ready[0], val(pe, blk + (1 + NB * ps), 1))
                    M.transpose(p_tr[:, 0:D], z1[:, :], ident[:, :]).then_inc(z1_t, 1)
                    pe.wait_ge(z1_tc, turn1)
                    for c in range(MC):
                        last = M.matmul(p_mlp[:, c * P:(c + 1) * P], w1[ps - 1][:, c * P:(c + 1) * P], lhs[:, :], start=True, stop=True)
                    last.then_inc(mlp1, 1)
                    pe.wait_ge(gelued, val(pe, blk * MC + (MC + MC * NB * (ps - 1)), 1))
                    for c in range(MC):
                        last = M.matmul(p_lin[:, 0:D], geluT[:, c, :], w2[ps - 1][:, c, :], start=(c == 0), stop=(c == MC - 1))
                    last.then_inc(mlp2, 1)

                def after_mlp(blk):
                    if ps == 1:
                        table_stage(1, val(pe, blk + (1 + NB * ps), 1))

                def finish(blk):
                    pass

                for k in range(4):
                    slots(0, k)
                aggregates(0)
                with pe.Fori(1, NB) as blk:
                    for k, tail in enumerate((transposed, mlp, after_mlp, finish)):
                        slots(blk, k)
                        tail(blk - 1)
                    aggregates(blk)
                for tail in (transposed, mlp, after_mlp, finish):
                    tail(NB - 1)


_INS = ['x', 'src', 'dst', 'edge_weight', 'L0_gnn_W', 'L0_gnn_b', 'L1_gnn_ln1_g', 'L1_gnn_ln1_b', 'L1_gnn_W_pre',
        'L1_gnn_b_pre', 'L1_gnn_W_post', 'L1_gnn_b_post', 'L1_gnn_W_lin', 'L1_gnn_b_lin', 'L1_gnn_ln2_g',
        'L1_gnn_ln2_b', 'L1_gnn_W1', 'L1_gnn_b1', 'L1_gnn_W2', 'L1_gnn_b2']


def kernel(**inputs):
    import numpy as _np
    import concourse.bacc as _bacc
    from concourse import mybir as _mybir
    from concourse.bass_utils import run_bass_kernel_spmd as _run

    nc = _bacc.Bacc("TRN2", target_bir_lowering=False, num_devices=1)
    arrays, args = {}, []
    for name in _INS:
        a = _np.ascontiguousarray(inputs[name])
        arrays[f"in_{name}_dram"] = a
        args.append(nc.dram_tensor(f"in_{name}_dram", a.shape, _mybir.dt.from_np(a.dtype), kind="ExternalInput").ap())
    out = nc.dram_tensor("out_0_dram", inputs["x"].shape, _mybir.dt.float32, kind="ExternalOutput").ap()
    gnn_kernel(nc, *args, out)
    r = _run(nc, [arrays], core_ids=[0])
    return r.results[0]["out_0_dram"]
```
